# Optimizing a Trainium2 kernel written in Bass

```python
import numpy as np
import jax
import jax.numpy as jnp

def _softmax(x, axis=-1):
    return jax.nn.softmax(x, axis=axis)

def _gelu(x):
    return jax.nn.gelu(x, approximate=True)

def _silu(x):
    return jax.nn.silu(x)

def _sigmoid(x):
    return jax.nn.sigmoid(x)

def _layernorm(x, axis=-1, eps=1e-05):
    m = jnp.mean(x, axis=axis, keepdims=True)
    v = jnp.var(x, axis=axis, keepdims=True)
    return (x - m) / jnp.sqrt(v + eps)

def _scatter_add(tgt, idx, src, axis=0):
    return tgt.at[idx].add(src)

def _segment_sum(src, seg, n):
    return jax.ops.segment_sum(src, seg, n)
kernel_name = 'mk_cond_resid_d4_seqx_r8_f88727'

def setup_inputs(seed: int=0):
    np.random.seed(seed)
    _w = jnp.asarray

    def _rec_inputs():
        import jax
        import jax.numpy as jnp
        _rk = jax.random.key(seed)
        x = -0.000125 + 0.9999 * jax.random.normal(jax.random.fold_in(_rk, 1), (8, 128, 512), jnp.float32)
        _lenS = 128 - jax.random.randint(jax.random.fold_in(_rk, 7), (8,), 0, max(1, 128 // 4) + 1, jnp.int32)
        _lenS2 = 128 - jax.random.randint(jax.random.fold_in(_rk, 8), (8,), 0, max(1, 128 // 4) + 1, jnp.int32)
        itok_B_6_15 = jax.random.randint(jax.random.fold_in(_rk, 11), (8,), 6, 16, jnp.int32)
        itok_B_0_15 = jax.random.randint(jax.random.fold_in(_rk, 12), (8,), 0, 16, jnp.int32)
        itok_B_9_3973 = jax.random.randint(jax.random.fold_in(_rk, 13), (8,), 9, 3974, jnp.int32)
        itok_B_1_7 = jax.random.randint(jax.random.fold_in(_rk, 14), (8,), 1, 8, jnp.int32)
        return (x, itok_B_6_15, itok_B_0_15, itok_B_9_3973, itok_B_1_7)
    x, itok_B_6_15, itok_B_0_15, itok_B_9_3973, itok_B_1_7 = _rec_inputs()

    def _L0_cond_setup():
        import jax, jax.numpy as jnp
        import numpy as np
        B, S, D_IN, D_OUT = (4, 256, 512, 512)
        RANK, MAX_LORAS = (16, 32)
        key = jax.random.key(seed)
        ks = jax.random.split(key, 6)
        x = jax.random.normal(ks[0], (B, S, D_IN), dtype=jnp.float32)
        adapter_ids = jax.random.randint(ks[1], (B,), 0, MAX_LORAS)
        base_weight = jax.random.normal(ks[2], (D_OUT, D_IN), dtype=jnp.float32) * D_IN ** (-0.5)
        base_bias = jax.random.normal(ks[3], (D_OUT,), dtype=jnp.float32) * 0.01
        lora_A_w = jax.random.normal(ks[4], (MAX_LORAS, RANK, D_IN), dtype=jnp.float32) * D_IN ** (-0.5)
        lora_B_w = jax.random.normal(ks[5], (MAX_LORAS, D_OUT, RANK), dtype=jnp.float32) * RANK ** (-0.5)
        return {'x': x, 'adapter_ids': adapter_ids, 'base_weight': base_weight, 'base_bias': base_bias, 'lora_A_w': lora_A_w, 'lora_B_w': lora_B_w}
    _L0_cond_all = _L0_cond_setup()
    _L0_cond_in = {k: v for k, v in _L0_cond_all.items() if k in ('base_weight', 'base_bias', 'lora_A_w', 'lora_B_w')}
    del _L0_cond_all

    def _L1_cond_setup():
        import jax, jax.numpy as jnp
        import numpy as np
        MAX_LORAS = 16
        IN, OUT = (512, 512)
        B, S = (8, 256)
        key = jax.random.key(seed)
        k1, k2, k3 = jax.random.split(key, 3)
        x = jax.random.normal(k1, (B, S, IN), dtype=jnp.float32)
        adapter_ids = jax.random.randint(k2, (B,), 0, MAX_LORAS)
        weight = jax.random.normal(k3, (MAX_LORAS, OUT, IN), dtype=jnp.float32) * 0.02
        return {'x': x, 'adapter_ids': adapter_ids, 'weight': weight}
    _L1_cond_all = _L1_cond_setup()
    _L1_cond_in = {k: v for k, v in _L1_cond_all.items() if k in ('weight',)}
    del _L1_cond_all

    def _L2_cond_setup():
        import jax, jax.numpy as jnp
        import numpy as np
        from jax import lax
        B, E, T = (32, 64, 512)
        K = 5
        PAD = (K - 1) // 2
        key = jax.random.key(seed)
        k1, k2, k3 = jax.random.split(key, 3)
        x = jax.random.normal(k1, (B, E, T), dtype=jnp.float32)
        length = jax.random.randint(k2, (B,), 1, T + 1, dtype=jnp.int64)
        conv_w = jax.random.normal(k3, (1, 1, K), dtype=jnp.float32) * (1.0 / np.sqrt(K))
        return {'x': x, 'length': length, 'conv_w': conv_w}
    _L2_cond_all = _L2_cond_setup()
    _L2_cond_in = {k: v for k, v in _L2_cond_all.items() if k in ('conv_w',)}
    del _L2_cond_all

    def _L3_cond_setup():
        import jax, jax.numpy as jnp
        import numpy as np
        B, S, D_IN, D_OUT = (4, 256, 512, 512)
        N_ADAPTERS, MAX_RANK = (8, 16)
        key = jax.random.key(seed)
        ks = jax.random.split(key, 7)
        x = jax.random.normal(ks[0], (B, S, D_IN), dtype=jnp.float32)
        weight = jax.random.normal(ks[1], (D_OUT, D_IN), dtype=jnp.float32) * (1.0 / np.sqrt(D_IN))
        bias = jax.random.normal(ks[2], (D_OUT,), dtype=jnp.float32) * 0.01
        lora_a_weights = jax.random.normal(ks[3], (N_ADAPTERS, MAX_RANK, D_IN), dtype=jnp.float32) * (1.0 / np.sqrt(D_IN))
        lora_b_weights = jax.random.normal(ks[4], (N_ADAPTERS, D_OUT, MAX_RANK), dtype=jnp.float32) * 0.02
        scaling_factors = jax.random.uniform(ks[5], (N_ADAPTERS,), dtype=jnp.float32, minval=0.5, maxval=2.0)
        adapter_id = jax.random.randint(ks[6], (B,), 0, N_ADAPTERS, dtype=jnp.int64)
        return {'x': x, 'weight': weight, 'bias': bias, 'lora_a_weights': lora_a_weights, 'lora_b_weights': lora_b_weights, 'scaling_factors': scaling_factors, 'adapter_id': adapter_id}
    _L3_cond_all = _L3_cond_setup()
    _L3_cond_in = {k: v for k, v in _L3_cond_all.items() if k in ('weight', 'bias', 'lora_a_weights', 'lora_b_weights', 'scaling_factors')}
    del _L3_cond_all
    return {'x': x, 'itok_B_6_15': itok_B_6_15, 'itok_B_0_15': itok_B_0_15, 'itok_B_9_3973': itok_B_9_3973, 'itok_B_1_7': itok_B_1_7, 'L0_cond_base_weight': _L0_cond_in['base_weight'], 'L0_cond_base_bias': _L0_cond_in['base_bias'], 'L0_cond_lora_A_w': _L0_cond_in['lora_A_w'], 'L0_cond_lora_B_w': _L0_cond_in['lora_B_w'], 'L1_cond_weight': _L1_cond_in['weight'], 'L2_cond_conv_w': _L2_cond_in['conv_w'], 'L3_cond_weight': _L3_cond_in['weight'], 'L3_cond_bias': _L3_cond_in['bias'], 'L3_cond_lora_a_weights': _L3_cond_in['lora_a_weights'], 'L3_cond_lora_b_weights': _L3_cond_in['lora_b_weights'], 'L3_cond_scaling_factors': _L3_cond_in['scaling_factors']}

def reference(x, itok_B_6_15, itok_B_0_15, itok_B_9_3973, itok_B_1_7, L0_cond_base_weight, L0_cond_base_bias, L0_cond_lora_A_w, L0_cond_lora_B_w, L1_cond_weight, L2_cond_conv_w, L3_cond_weight, L3_cond_bias, L3_cond_lora_a_weights, L3_cond_lora_b_weights, L3_cond_scaling_factors):
    import jax
    import jax.numpy as jnp

    def _L0_cond_ref(x, adapter_ids, base_weight, base_bias, lora_A_w, lora_B_w):
        import jax, jax.numpy as jnp
        import numpy as np
        B, S, D_IN, D_OUT = (4, 256, 512, 512)
        RANK, MAX_LORAS = (16, 32)
        result = jnp.einsum('bsd,od->bso', x, base_weight) + base_bias
        A = lora_A_w[adapter_ids]
        Bw = lora_B_w[adapter_ids]
        h = jnp.einsum('bsd,brd->bsr', x, A)
        lora_out = jnp.einsum('bsr,bor->bso', h, Bw)
        result = result + lora_out
        return result.astype(x.dtype)

    def _L1_cond_ref(x, adapter_ids, weight):
        import jax, jax.numpy as jnp
        import numpy as np
        MAX_LORAS = 16
        IN, OUT = (512, 512)
        B, S = (8, 256)
        w = weight[adapter_ids]
        return jnp.einsum('bsi,boi->bso', x, w)

    def _L2_cond_ref(x, length, conv_w):
        import jax, jax.numpy as jnp
        import numpy as np
        from jax import lax
        B, E, T = (32, 64, 512)
        K = 5
        PAD = (K - 1) // 2
        mask = (jnp.arange(T)[None, :] < length[:, None]).astype(x.dtype)
        denom = length.astype(x.dtype)[:, None]
        y = jnp.einsum('bet,bt->be', x, mask) / denom
        yc = lax.conv_general_dilated(y[:, None, :], conv_w, window_strides=(1,), padding=[(PAD, PAD)], dimension_numbers=('NCH', 'OIH', 'NCH'))[:, 0, :]
        gate = jax.nn.sigmoid(yc)
        return x * gate[:, :, None]

    def _L3_cond_ref(x, weight, bias, lora_a_weights, lora_b_weights, scaling_factors, adapter_id):
        import jax, jax.numpy as jnp
        import numpy as np
        B, S, D_IN, D_OUT = (4, 256, 512, 512)
        N_ADAPTERS, MAX_RANK = (8, 16)
        base = jnp.einsum('bsi,oi->bso', x, weight) + bias
        a_sel = lora_a_weights[adapter_id]
        b_sel = lora_b_weights[adapter_id]
        scale = scaling_factors[adapter_id]
        low = jnp.einsum('bsi,bri->bsr', x, a_sel)
        delta = jnp.einsum('bsr,bor->bso', low, b_sel)
        return base + scale[:, None, None] * delta
    x = x + _L0_cond_ref(x, itok_B_6_15, L0_cond_base_weight, L0_cond_base_bias, L0_cond_lora_A_w, L0_cond_lora_B_w)
    x = x + _L1_cond_ref(x, itok_B_0_15, L1_cond_weight)
    x = x + _L2_cond_ref(x, itok_B_9_3973, L2_cond_conv_w)
    x = x + _L3_cond_ref(x, L3_cond_weight, L3_cond_bias, L3_cond_lora_a_weights, L3_cond_lora_b_weights, L3_cond_scaling_factors, itok_B_1_7)
    return x

_drawn_inputs = setup_inputs


def setup_inputs(seed=0):
    import zlib

    import numpy as np

    out = dict(_drawn_inputs(seed))
    spreads = {}
    factors = {'L0_cond_base_bias': 8.0,
     'L2_cond_conv_w': 4.502,
     'L3_cond_bias': 24.372,
     'L3_cond_scaling_factors': 3.035}
    for name, (base, spread) in spreads.items():
        noise = np.random.default_rng([zlib.crc32(name.encode()), seed]).standard_normal(out[name].shape)
        drawn = base * np.exp(spread * noise) if base else spread * noise
        out[name] = jnp.asarray(drawn.astype(out[name].dtype))
    for name, factor in factors.items():
        out[name] = (out[name] * factor).astype(out[name].dtype)
    return out
```

```python
from contextlib import ExitStack

import concourse.bass as bass
from concourse import mybir
from concourse.alu_op_type import AluOpType as ALU

ACT = mybir.ActivationFunctionType
F32 = mybir.dt.float32
F32R = mybir.dt.float32r
I32 = mybir.dt.int32

P = 128
B, S, D = 8, 128, 512
C = D // P
R = 16
TAPS = 5
HALO = (TAPS - 1) // 2
G = 32
LOW = 3 * G
DMA = 16


class Batch:

    def __init__(self, index, rounds, slot):
        self.index, self.rounds, self.slot = index, rounds, slot
        self.is_first = isinstance(index, int) and index == 0
        self.in_first_pair = isinstance(index, int) and index < 2

    def shift(self, by):
        moved = self.slot + by
        return Batch(self.index + by, self.rounds + moved // 2, moved % 2)


def fixed(n):
    return Batch(n, n // 2, n % 2)


def in_pair(pair, member):
    return Batch(2 * pair, pair, 0).shift(member)


def layers_kernel(nc, xT, len_dram, id0, id1, id3, w0T, bias0, a0T, b0T, w1T, conv_w, w3T, bias3, a3T, b3T, scales, out):
    ctx = ExitStack()
    with ctx:
        def sb(name, shape, dt=F32):
            return ctx.enter_context(nc.sbuf_tensor(name, shape, dt))

        def psum(name):
            return ctx.enter_context(nc.psum_tensor(name, [P, D], F32))

        def sem(name):
            return ctx.enter_context(nc.semaphore(name))

        def sems(name, n):
            return [sem(f"{name}_{k}") for k in range(n)]

        x_raw = sb("x_raw", [P, 2, D])
        w0_raw = sb("w0_raw", [P, C, D])
        w1_raw = sb("w1_raw", [P, 2, C * D])
        w3_raw = sb("w3_raw", [P, C, D])
        a_raw = [sb(f"a{n}_raw", [P, 2, C, R]) for n in (0, 3)]
        b_raw = [sb(f"b{n}_raw", [P, 2, D]) for n in (0, 3)]
        scale = sb("scale", [P, 2])
        xT_hi, xT_lo = sb("xT_hi", [P, 2, D], F32R), sb("xT_lo", [P, 2, D], F32R)
        x1T_hi, x1T_lo = sb("x1T_hi", [P, D], F32R), sb("x1T_lo", [P, D], F32R)
        x2T_hi, x2T_lo = sb("x2T_hi", [P, D], F32R), sb("x2T_lo", [P, D], F32R)
        w0_hi, w0_lo = sb("w0_hi", [P, C, D], F32R), sb("w0_lo", [P, C, D], F32R)
        w1_hi, w1_lo = sb("w1_hi", [P, 2, C * D], F32R), sb("w1_lo", [P, 2, C * D], F32R)
        w3_hi, w3_lo = sb("w3_hi", [P, C, D], F32R), sb("w3_lo", [P, C, D], F32R)
        a_cat = [sb(f"a{n}_cat", [P, 2, C, 3, 2, R], F32R) for n in (0, 3)]
        b_cat = [sb(f"b{n}_cat", [P, 2, D], F32R) for n in (0, 3)]
        h_cat = [sb(f"h{n}_cat", [P, S], F32R) for n in (0, 3)]
        x1 = sb("x1", [P, 2, D])
        x2 = sb("x2", [P, D])
        masked = sb("masked", [P, D])
        x4 = sb("x4", [P, 2, D])
        identity_halo = sb("identity_halo", [P, P + 2 * HALO])
        identity = identity_halo[:, HALO:HALO + P]
        position = sb("position", [P, D])
        conv_taps = sb("conv_taps", [P, TAPS])
        band = sb("band", [P, P])
        bias3_rows = sb("bias3_rows", [P, D])
        bias0_raw = sb("bias0_raw", [P, D])
        bias0_hi = sb("bias0_hi", [P, D], F32R)
        bias0_lo = sb("bias0_lo", [P, D])
        length_int = sb("length_int", [P, B], I32)
        length = sb("length", [P, B])
        inv_length = sb("inv_length", [P, B])
        row_sum = sb("row_sum", [P, 1])
        gate = sb("gate", [P, 1])
        zero = sb("zero", [P, 1])
        gate_plus_1 = sb("gate_plus_1", [P, 1])

        ps_l0, ps_l1, ps_l3 = psum("ps_l0"), psum("ps_l1"), psum("ps_l3")
        ps_x1T, ps_x2T = psum("ps_x1T"), psum("ps_x2T")
        ps_low = [psum("ps_low0"), psum("ps_low3")]
        ps_conv = psum("ps_conv")

        x_loaded, w1_loaded = sems("x_loaded", 2), sems("w1_loaded", 2)
        ab_loaded = [sems("ab0_loaded", 2), sems("ab3_loaded", 2)]
        w0_loaded, w3_loaded = sems("w0_loaded", C), sem("w3_loaded")
        bias0_loaded, small_loaded, bias3_loaded = sem("bias0_loaded"), sem("small_loaded"), sem("bias3_loaded")
        stored = sems("stored", 2)
        identity_zeroed, identity_ready, position_ready = sem("identity_zeroed"), sem("identity_ready"), sem("position_ready")
        h0_static, zero_ready = sem("h0_static"), sem("zero_ready")
        bias0_step, bias0_ready = sem("bias0_step"), sem("bias0_ready")
        length_ready, inv_length_ready = sem("length_ready"), sem("inv_length_ready")
        band_step, w0_plus_i, w3_plus_i = sem("band_step"), sem("w0_plus_i"), sem("w3_plus_i")
        w0_hi_ready, w0_split, w3_hi_ready, w3_split = sem("w0_hi_ready"), sem("w0_split"), sem("w3_hi_ready"), sem("w3_split")
        xT_hi_ready, xT_split = sem("xT_hi_ready"), sem("xT_split")
        w1_hi_ready, w1_split = sem("w1_hi_ready"), sem("w1_split")
        a_hi_ready, b_hi_ready = [sem("a0_hi_ready"), sem("a3_hi_ready")], [sem("b0_hi_ready"), sem("b3_hi_ready")]
        ab_split = [sem("ab0_split"), sem("ab3_split")]
        low_done = [sem("low0_done"), sem("low3_done")]
        h_hi_ready, h_split = [sem("h0_hi_ready"), sem("h3_hi_ready")], [sem("h0_split"), sem("h3_split")]
        l0_done, l1_done, l3_done = sem("l0_done"), sem("l1_done"), sem("l3_done")
        x1_ready, x2_ready = sem("x1_ready"), sem("x2_ready")
        x1T_done, x1T_hi_ready, x1T_split = sem("x1T_done"), sem("x1T_hi_ready"), sem("x1T_split")
        x2T_done, x2T_hi_ready, x2T_split = sem("x2T_done"), sem("x2T_hi_ready"), sem("x2T_split")
        row_sum_ready, conv_done, gate_ready, gate_plus_ready = sem("row_sum_ready"), sem("conv_done"), sem("gate_ready"), sem("gate_plus_ready")
        x4_ready = sem("x4_ready")

        AB_LOADS = [4, 5]
        W1_HALVES = [slice(k * C * D // 2, (k + 1) * C * D // 2) for k in range(2)]

        block = ctx.enter_context(nc.Block())

        @block.sync
        def _(sp):
            def load_x(b):
                if not b.in_first_pair:
                    sp.wait_ge(xT_split, b.index - 1)
                sp.dma_start(x_raw[:, b.slot, :], xT[bass.ds(b.index, 1), :, :].rearrange("b p n -> (b p) n")).then_inc(x_loaded[b.slot], DMA)

            def load_w1(b):
                which = sp.value_load(id1[0:1, bass.ds(b.index, 1)], min_val=0, max_val=w1T.shape[0] - 1)
                if not b.in_first_pair:
                    sp.wait_ge(w1_split, 2 * (b.index - 1))
                sp.dma_start(w1_raw[:, b.slot, :], w1T[bass.ds(which, 1), :, :].rearrange("b p n -> (b p) n")).then_inc(w1_loaded[b.slot], DMA)

            def load_ab(b, n):
                ids, a_dram, b_dram = ((id0, a0T, b0T), (id3, a3T, b3T))[n]
                which = sp.value_load(ids[0:1, bass.ds(b.index, 1)], min_val=0, max_val=a_dram.shape[0] - 1)
                if not b.in_first_pair:
                    sp.wait_ge(ab_split[n], 2 * (b.index - 1))
                    if n == 1:
                        sp.wait_ge(h_split[1], b.index - 1)
                landed = ab_loaded[n][b.slot]
                sp.dma_start(a_raw[n][:, b.slot, :, :].rearrange("p c r -> p (c r)"),
                             a_dram[bass.ds(which, 1), :, :].rearrange("b p n -> (b p) n")).then_inc(landed, DMA)
                for g in range(3):
                    sp.dma_start(b_raw[n][g * G:(g + 1) * G, b.slot, :],
                                 b_dram[bass.ds(which, 1), :, :].rearrange("b r n -> (b r) n")).then_inc(landed, DMA)
                if n == 1:
                    sp.dma_start(scale[:, b.slot:b.slot + 1], scales[0:1, bass.ds(which, 1)].partition_broadcast(P)).then_inc(landed, DMA)

            load_x(fixed(0))
            for c in range(C):
                sp.dma_start(w0_raw[:, c, :], w0T[:, c * D:(c + 1) * D]).then_inc(w0_loaded[c], DMA)
            load_ab(fixed(0), 0)
            load_w1(fixed(0))
            sp.dma_start(bias0_raw[LOW:LOW + 1, :], bias0).then_inc(bias0_loaded, DMA)
            sp.dma_start(bias0_raw[LOW + 1:LOW + 2, :], bias0).then_inc(bias0_loaded, DMA)
            sp.dma_start(length_int[:, :], len_dram.partition_broadcast(P)).then_inc(small_loaded, DMA)
            sp.dma_start(conv_taps[:, :], conv_w.partition_broadcast(P)).then_inc(small_loaded, DMA)
            load_x(fixed(1))
            load_ab(fixed(1), 0)
            load_w1(fixed(1))
            sp.dma_start(w3_raw[:, :, :].rearrange("p c n -> p (c n)"), w3T).then_inc(w3_loaded, DMA)
            sp.dma_start(bias3_rows[:, :], bias3.partition_broadcast(P)).then_inc(bias3_loaded, DMA)
            load_ab(fixed(0), 1)
            load_ab(fixed(1), 1)
            with sp.Fori(1, B // 2) as j:
                for slot in range(2):
                    b = in_pair(j, slot)
                    load_x(b)
                    load_ab(b, 0)
                    load_w1(b)
                    load_ab(b, 1)

        @block.gpsimd
        def _(pool):
            nc.gpsimd.memset(zero[:, :], 0.0).then_inc(zero_ready, 1)
            nc.gpsimd.memset(identity_halo[:, :], 0.0).then_inc(identity_zeroed, 1)
            pool.wait_ge(identity_zeroed, 1)
            nc.gpsimd.affine_select(out=identity_halo[:, :], in_=identity_halo[:, :], compare_op=ALU.not_equal, fill=1.0,
                                    base=HALO, pattern=[[-1, P + 2 * HALO]], channel_multiplier=1).then_inc(identity_ready, 1)
            nc.gpsimd.iota(position[:, :], pattern=[[1, D]], base=0, channel_multiplier=0,
                           allow_small_or_imprecise_dtypes=True).then_inc(position_ready, 1)

            def split_ab(b, n):
                a_in = a_raw[n][:, b.slot, :, :].unsqueeze(2).broadcast_to([P, C, 3, R])
                a_hi, a_lo = a_cat[n][:, b.slot, :, :, 0, :], a_cat[n][:, b.slot, :, :, 1, :]
                b_in, b_out = b_raw[n][0:LOW, b.slot, :], b_cat[n][0:LOW, b.slot, :]
                pool.wait_ge(ab_loaded[n][b.slot], DMA * AB_LOADS[n] * (b.rounds + 1))
                if not b.in_first_pair:
                    pool.wait_ge((l0_done, l3_done)[n], b.index - 1)
                nc.gpsimd.tensor_tensor(a_hi, a_in, zero[:, :].unsqueeze(2).unsqueeze(3).broadcast_to([P, C, 3, R]), ALU.add).then_inc(a_hi_ready[n], 1)
                nc.gpsimd.tensor_copy(b_out, b_in).then_inc(b_hi_ready[n], 1)
                pool.wait_ge(a_hi_ready[n], b.index + 1)
                nc.gpsimd.tensor_tensor(a_lo, a_in, a_hi.bitcast(F32), ALU.subtract).then_inc(ab_split[n], 1)
                pool.wait_ge(b_hi_ready[n], b.index + 1)
                nc.gpsimd.tensor_tensor(b_out[0:G, :], b_in[0:G, :], b_out[0:G, :].bitcast(F32),
                                        ALU.subtract).then_inc(ab_split[n], 1)

            pool.wait_ge(zero_ready, 1)
            split_ab(fixed(0), 0)
            split_ab(fixed(1), 0)
            split_ab(fixed(0), 1)
            split_ab(fixed(1), 1)
            with pool.Fori(1, B // 2) as j:
                for slot in range(2):
                    for n in range(2):
                        split_ab(in_pair(j, slot), n)

        @block.scalar
        def _(act):
            def x_hi(b):
                act.wait_ge(x_loaded[b.slot], DMA * (b.rounds + 1))
                if not b.in_first_pair:
                    act.wait_ge(l0_done, b.index - 1)
                nc.scalar.copy(xT_hi[:, b.slot, :], x_raw[:, b.slot, :]).then_inc(xT_hi_ready, 1)

            def w1_hi_half(b, half):
                if half == 0:
                    act.wait_ge(w1_loaded[b.slot], DMA * (b.rounds + 1))
                    if not b.in_first_pair:
                        act.wait_ge(l1_done, b.index - 1)
                cols = W1_HALVES[half]
                nc.scalar.copy(w1_hi[:, b.slot, cols], w1_raw[:, b.slot, cols]).then_inc(w1_hi_ready, 1)

            def h0_hi(b):
                act.wait_ge(low_done[0], b.index + 1)
                nc.scalar.copy(h_cat[0][0:LOW, :], ps_low[0][0:LOW, 0:S]).then_inc(h_hi_ready[0], 1)

            def h3_hi(b):
                act.wait_ge(low_done[1], b.index + 1)
                act.wait_ge(ab_loaded[1][b.slot], DMA * AB_LOADS[1] * (b.rounds + 1))
                nc.scalar.activation(h_cat[1][0:LOW, :], ps_low[1][0:LOW, 0:S], ACT.Copy,
                                     scale=scale[0:LOW, b.slot:b.slot + 1]).then_inc(h_hi_ready[1], 1)

            def copy_x1(b):
                act.wait_ge(l0_done, b.index + 1)
                if not b.in_first_pair:
                    act.wait_ge(x2_ready, b.index - 1)
                nc.scalar.copy(x1[:, b.slot, :], ps_l0[:, :]).then_inc(x1_ready, 1)

            def x1T_hi_part(b):
                act.wait_ge(x1T_done, b.index + 1)
                if not b.is_first:
                    act.wait_ge(l1_done, b.index)
                nc.scalar.copy(x1T_hi[:, :], ps_x1T[:, :]).then_inc(x1T_hi_ready, 1)

            def x2T_hi_part(b):
                act.wait_ge(x2T_done, b.index + 1)
                if not b.is_first:
                    act.wait_ge(l3_done, b.index)
                nc.scalar.copy(x2T_hi[:, :], ps_x2T[:, :]).then_inc(x2T_hi_ready, 1)

            def gate_rows(b):
                act.wait_ge(conv_done, b.index + 1)
                if not b.is_first:
                    act.wait_ge(gate_plus_ready, b.index)
                nc.scalar.activation(gate[:, :], ps_conv[:, 0:1], ACT.Sigmoid,
                                     scale=inv_length[:, bass.ds(b.index, 1)]).then_inc(gate_ready, 1)

            def store(b):
                act.wait_ge(x4_ready, b.index + 1)
                act.dma_start(out[bass.ds(b.index, 1), :, :].rearrange("b s n -> (b s) n"), x4[:, b.slot, :]).then_inc(stored[b.slot], DMA)

            x_hi(fixed(0))
            for c in range(C):
                act.wait_ge(w0_plus_i, c + 1)
                nc.scalar.copy(w0_hi[:, c, :], w0_raw[:, c, :]).then_inc(w0_hi_ready, 1)
            h0_hi(fixed(0))
            w1_hi_half(fixed(0), 0)
            copy_x1(fixed(0))
            w1_hi_half(fixed(0), 1)
            x1T_hi_part(fixed(0))
            x_hi(fixed(1))
            w1_hi_half(fixed(1), 0)
            w1_hi_half(fixed(1), 1)
            for c in range(C):
                act.wait_ge(w3_plus_i, c + 1)
                nc.scalar.copy(w3_hi[:, c, :], w3_raw[:, c, :]).then_inc(w3_hi_ready, 1)

            act.wait_ge(inv_length_ready, 1)

            def step(b, last=False):
                before, after = b.shift(-1), b.shift(1)
                h0_hi(b)
                x2T_hi_part(before)
                copy_x1(b)
                gate_rows(before)
                h3_hi(before)
                if not last:
                    w1_hi_half(after, 0)
                x1T_hi_part(b)
                if not last:
                    x_hi(after)
                    w1_hi_half(after, 1)
                store(before)

            step(fixed(1))
            step(fixed(2))
            with act.Fori(1, B // 2 - 1) as j:
                for member in range(2):
                    step(in_pair(j, 1 + member))
            step(fixed(B - 1), last=True)
            x2T_hi_part(fixed(B - 1))
            gate_rows(fixed(B - 1))
            h3_hi(fixed(B - 1))
            store(fixed(B - 1))
            for slot in range(2):
                act.wait_ge(stored[slot], DMA * (B // 2))

        @block.vector
        def _(dve):
            def subtract(out_, full, hi):
                return nc.vector.tensor_tensor(out_, full, hi.bitcast(F32), ALU.subtract)

            def x_lo(b):
                dve.wait_ge(xT_hi_ready, b.index + 1)
                subtract(xT_lo[:, b.slot, :], x_raw[:, b.slot, :], xT_hi[:, b.slot, :]).then_inc(xT_split, 1)

            def w1_lo_half(b, half):
                cols = W1_HALVES[half]
                dve.wait_ge(w1_hi_ready, 2 * b.index + half + 1)
                subtract(w1_lo[:, b.slot, cols], w1_raw[:, b.slot, cols], w1_hi[:, b.slot, cols]).then_inc(w1_split, 1)

            def h0_lo(b):
                dve.wait_ge(h_hi_ready[0], b.index + 1)
                subtract(h_cat[0][2 * G:LOW, :], ps_low[0][2 * G:LOW, 0:S], h_cat[0][2 * G:LOW, :]).then_inc(h_split[0], 1)

            def h3_lo(b):
                dve.wait_ge(h_hi_ready[1], b.index + 1)
                nc.vector.scalar_tensor_tensor(out=h_cat[1][2 * G:LOW, :], in0=ps_low[1][2 * G:LOW, 0:S],
                                               scalar=scale[2 * G:LOW, b.slot:b.slot + 1], in1=h_cat[1][2 * G:LOW, :].bitcast(F32),
                                               op0=ALU.mult, op1=ALU.subtract).then_inc(h_split[1], 1)

            def x1T_lo_part(b):
                dve.wait_ge(x1T_hi_ready, b.index + 1)
                subtract(x1T_lo[:, :], ps_x1T[:, :], x1T_hi[:, :]).then_inc(x1T_split, 1)

            def x2T_lo_part(b):
                dve.wait_ge(x2T_hi_ready, b.index + 1)
                subtract(x2T_lo[:, :], ps_x2T[:, :], x2T_hi[:, :]).then_inc(x2T_split, 1)

            def sum_x2(b):
                dve.wait_ge(l1_done, b.index + 1)
                if not b.is_first:
                    dve.wait_ge(x2T_done, b.index)
                    dve.wait_ge(row_sum_ready, b.index)
                nc.vector.tensor_tensor(x2[:, :], ps_l1[:, :], x1[:, b.slot, :], ALU.add).then_inc(x2_ready, 1)
                dve.wait_ge(x2_ready, b.index + 1)
                if not b.is_first:
                    dve.wait_ge(conv_done, b.index)
                nc.vector.scalar_tensor_tensor(out=masked[:, :], in0=position[:, :], scalar=length[:, bass.ds(b.index, 1)], in1=x2[:, :],
                                               op0=ALU.is_lt, op1=ALU.mult, accum_out=row_sum[:, :]).then_inc(row_sum_ready, 1)

            def add_1_to_gate(b):
                dve.wait_ge(gate_ready, b.index + 1)
                if not b.is_first:
                    dve.wait_ge(x4_ready, b.index)
                nc.vector.tensor_scalar(gate_plus_1[:, :], gate[:, :], 1.0, None, ALU.add).then_inc(gate_plus_ready, 1)

            def result(b):
                dve.wait_ge(l3_done, b.index + 1)
                dve.wait_ge(gate_plus_ready, b.index + 1)
                if not b.in_first_pair:
                    dve.wait_ge(stored[b.slot], DMA * b.rounds)
                nc.vector.scalar_tensor_tensor(out=x4[:, b.slot, :], in0=ps_l3[:, :], scalar=gate_plus_1[:, 0:1], in1=bias3_rows[:, :],
                                               op0=ALU.mult, op1=ALU.add).then_inc(x4_ready, 1)

            def add_identity(w_raw, done):
                for c in range(C):
                    if done is w0_plus_i:
                        dve.wait_ge(w0_loaded[c], DMA)
                    diagonal = w_raw[:, c, c * P:(c + 1) * P]
                    nc.vector.tensor_tensor(diagonal, diagonal, identity, ALU.add).then_inc(done, 1)
                    yield c

            x_lo(fixed(0))
            dve.wait_ge(identity_ready, 1)

            def w_lo(c, w_lo_, w_raw, w_hi_, hi_ready, split):
                dve.wait_ge(hi_ready, c + 1)
                subtract(w_lo_[:, c, :], w_raw[:, c, :], w_hi_[:, c, :]).then_inc(split, 1)

            for c in add_identity(w0_raw, w0_plus_i):
                if c:
                    w_lo(c - 1, w0_lo, w0_raw, w0_hi, w0_hi_ready, w0_split)
            w_lo(C - 1, w0_lo, w0_raw, w0_hi, w0_hi_ready, w0_split)

            nc.vector.memset(h_cat[0][LOW:P, :].bitcast(F32), 0.0).then_inc(h0_static, 1)
            dve.wait_ge(h0_static, 1)
            nc.vector.memset(h_cat[0][LOW:LOW + 2, :].bitcast(F32), 1.0).then_inc(h0_static, 1)
            rows = slice(LOW, LOW + 2)
            dve.wait_ge(bias0_loaded, 2 * DMA)
            nc.vector.tensor_copy(bias0_hi[rows, :], bias0_raw[rows, :]).then_inc(bias0_step, 1)
            dve.wait_ge(bias0_step, 1)
            subtract(bias0_lo[rows, :], bias0_raw[rows, :], bias0_hi[rows, :]).then_inc(bias0_step, 1)
            dve.wait_ge(bias0_step, 2)
            nc.vector.tensor_scalar(bias0_lo[rows, :], bias0_lo[rows, :], identity[rows, LOW + 1:LOW + 2], None, ALU.mult).then_inc(bias0_step, 1)
            for slot in range(2):
                nc.vector.memset(b_cat[0][LOW:P, slot, :].bitcast(F32), 0.0).then_inc(bias0_step, 1)
            dve.wait_ge(bias0_step, 5)
            for slot in range(2):
                nc.vector.scalar_tensor_tensor(out=b_cat[0][rows, slot, :], in0=bias0_hi[rows, :].bitcast(F32), scalar=identity[rows, LOW:LOW + 1],
                                               in1=bias0_lo[rows, :], op0=ALU.mult, op1=ALU.add).then_inc(bias0_ready, 1)

            h0_lo(fixed(0))
            w1_lo_half(fixed(0), 0)
            w1_lo_half(fixed(0), 1)
            x1T_lo_part(fixed(0))
            x_lo(fixed(1))
            dve.wait_ge(small_loaded, 2 * DMA)
            nc.vector.tensor_copy(length[:, :], length_int[:, :]).then_inc(length_ready, 1)
            dve.wait_ge(length_ready, 1)
            nc.vector.reciprocal(inv_length[:, :], length[:, :]).then_inc(inv_length_ready, 1)
            dve.wait_ge(position_ready, 1)
            sum_x2(fixed(0))
            w1_lo_half(fixed(1), 0)
            w1_lo_half(fixed(1), 1)
            for t in range(TAPS):
                ones_at = identity_halo[:, t:t + P]
                if t == 0:
                    nc.vector.tensor_scalar(band[:, :], ones_at, conv_taps[:, 0:1], None, ALU.mult).then_inc(band_step, 1)
                else:
                    dve.wait_ge(band_step, t)
                    nc.vector.scalar_tensor_tensor(out=band[:, :], in0=ones_at, scalar=conv_taps[:, t:t + 1], in1=band[:, :],
                                                   op0=ALU.mult, op1=ALU.add).then_inc(band_step, 1)
            dve.wait_ge(w3_loaded, DMA)
            for c in add_identity(w3_raw, w3_plus_i):
                pass
            for c in range(C):
                w_lo(c, w3_lo, w3_raw, w3_hi, w3_hi_ready, w3_split)
            dve.wait_ge(bias3_loaded, DMA)

            def step(b, last=False):
                before, after = b.shift(-1), b.shift(1)
                h0_lo(b)
                x2T_lo_part(before)
                h3_lo(before)
                if not last:
                    w1_lo_half(after, 0)
                x1T_lo_part(b)
                if not last:
                    x_lo(after)
                add_1_to_gate(before)
                result(before)
                if not last:
                    w1_lo_half(after, 1)
                sum_x2(b)

            step(fixed(1))
            step(fixed(2))
            with dve.Fori(1, B // 2 - 1) as j:
                for member in range(2):
                    step(in_pair(j, 1 + member))
            step(fixed(B - 1), last=True)
            x2T_lo_part(fixed(B - 1))
            h3_lo(fixed(B - 1))
            add_1_to_gate(fixed(B - 1))
            result(fixed(B - 1))

        @block.tensor
        def _(pe):
            def low_rank(b, n, hi, lo):
                pe.wait_ge(ab_split[n], 2 * (b.index + 1))
                for c in range(C):
                    a = a_cat[n][:, b.slot, c, :, :, :].rearrange("p g k r -> p (g k r)")
                    for k, part in enumerate((hi, lo)):
                        last = nc.tensor.matmul(ps_low[n][0:LOW, 0:S], a, part[:, c * P:(c + 1) * P],
                                                start=(c == 0 and k == 0), stop=(c == C - 1 and k == 1))
                last.then_inc(low_done[n], 1)

            def product(ps, chunks, hi, lo, w_hi_, w_lo_, last_stops=False):
                for c in chunks:
                    rows, cols = slice(c * P, (c + 1) * P), slice(c * D, (c + 1) * D)
                    nc.tensor.matmul(ps[:, :], hi[:, rows], w_hi_[:, cols], start=(c == 0), stop=False)
                    nc.tensor.matmul(ps[:, :], lo[:, rows], w_hi_[:, cols], start=False, stop=False)
                    last = nc.tensor.matmul(ps[:, :], hi[:, rows], w_lo_[:, cols], start=False, stop=(last_stops and c == C - 1))
                return last

            def add_low_rank(b, n, ps, rows):
                pe.wait_ge(h_split[n], b.index + 1)
                return nc.tensor.matmul(ps[:, :], h_cat[n][0:rows, :], b_cat[n][0:rows, b.slot, :], start=False, stop=True)

            def transposes(ps, rows, done):
                for c in range(C):
                    last = nc.tensor.transpose(ps[:, c * P:(c + 1) * P], rows[:, c * P:(c + 1) * P], identity)
                last.then_inc(done, 1)

            w0 = [w[:, :, :].rearrange("p c n -> p (c n)") for w in (w0_hi, w0_lo)]
            w3 = [w[:, :, :].rearrange("p c n -> p (c n)") for w in (w3_hi, w3_lo)]

            def transpose_x1(b):
                pe.wait_ge(x1_ready, b.index + 1)
                transposes(ps_x1T, x1[:, b.slot, :], x1T_done)

            def transpose_x2(b):
                pe.wait_ge(x2_ready, b.index + 1)
                transposes(ps_x2T, x2, x2T_done)

            def layer0(b, between):
                hi, lo = xT_hi[:, b.slot, :], xT_lo[:, b.slot, :]
                pe.wait_ge(xT_split, b.index + 1)
                low_rank(b, 0, hi, lo)
                product(ps_l0, range(C // 2), hi, lo, *w0)
                between()
                product(ps_l0, range(C // 2, C), hi, lo, *w0)
                add_low_rank(b, 0, ps_l0, P).then_inc(l0_done, 1)

            def layer3(b, between):
                pe.wait_ge(x2T_split, b.index + 1)
                pe.wait_ge(row_sum_ready, b.index + 1)
                if not b.is_first:
                    pe.wait_ge(gate_ready, b.index)
                nc.tensor.matmul(ps_conv[:, 0:1], band[:, :], row_sum[:, :], start=True, stop=True).then_inc(conv_done, 1)
                low_rank(b, 1, x2T_hi, x2T_lo)
                if not b.is_first:
                    pe.wait_ge(x4_ready, b.index)
                product(ps_l3, range(C // 2), x2T_hi, x2T_lo, *w3)
                between()
                product(ps_l3, range(C // 2, C), x2T_hi, x2T_lo, *w3)
                add_low_rank(b, 1, ps_l3, LOW).then_inc(l3_done, 1)

            def layer1(b):
                pe.wait_ge(x1T_split, b.index + 1)
                w1 = [w[:, b.slot, :] for w in (w1_hi, w1_lo)]
                for half in range(2):
                    pe.wait_ge(w1_split, 2 * b.index + half + 1)
                    last = product(ps_l1, range(half * C // 2, (half + 1) * C // 2), x1T_hi, x1T_lo, *w1, last_stops=True)
                last.then_inc(l1_done, 1)

            first = fixed(0)
            pe.wait_ge(xT_split, 1)
            for c in range(C):
                pe.wait_ge(w0_split, c + 1)
                product(ps_l0, [c], xT_hi[:, 0, :], xT_lo[:, 0, :], *w0)
            low_rank(first, 0, xT_hi[:, 0, :], xT_lo[:, 0, :])
            pe.wait_ge(h0_static, 2)
            pe.wait_ge(bias0_ready, 2)
            add_low_rank(first, 0, ps_l0, P).then_inc(l0_done, 1)
            transpose_x1(first)
            layer1(first)

            def step(b):
                before = b.shift(-1)
                layer0(b, lambda: transpose_x2(before))
                layer3(before, lambda: transpose_x1(b))
                layer1(b)

            pe.wait_ge(band_step, TAPS)
            pe.wait_ge(w3_split, C)
            step(fixed(1))
            step(fixed(2))
            with pe.Fori(1, B // 2 - 1) as j:
                for member in range(2):
                    step(in_pair(j, 1 + member))
            step(fixed(B - 1))
            last_batch = fixed(B - 1)
            transpose_x2(last_batch)
            layer3(last_batch, lambda: None)


def kernel(**inputs):
    import numpy as np
    import concourse.bacc as bacc
    from concourse.bass_utils import run_bass_kernel_spmd

    given = {name: np.asarray(a) for name, a in inputs.items()}

    def row(a):
        return a.reshape(1, -1)

    def features_first(w):
        *lead, rows, _ = w.shape
        w = w.reshape(*lead, rows, C, P)
        k = len(lead)
        return w.transpose(*range(k), k + 2, k + 1, k).reshape(*lead, P, C * rows)

    def rank_rows(w):
        w = w.transpose(0, 2, 1)
        return np.concatenate([w, w], axis=1)

    laid_out = {
        "xT": features_first(given["x"]),
        "lengths": row(given["itok_B_9_3973"]),
        "id0": row(given["itok_B_6_15"]),
        "id1": row(given["itok_B_0_15"]),
        "id3": row(given["itok_B_1_7"]),
        "w0T": features_first(given["L0_cond_base_weight"]),
        "bias0": row(given["L0_cond_base_bias"]),
        "a0T": features_first(given["L0_cond_lora_A_w"]),
        "b0T": rank_rows(given["L0_cond_lora_B_w"]),
        "w1T": features_first(given["L1_cond_weight"]),
        "conv_w": row(given["L2_cond_conv_w"]),
        "w3T": features_first(given["L3_cond_weight"]),
        "bias3": row(given["L3_cond_bias"]),
        "a3T": features_first(given["L3_cond_lora_a_weights"]),
        "b3T": rank_rows(given["L3_cond_lora_b_weights"]),
        "scales": row(given["L3_cond_scaling_factors"]),
    }
    nc = bacc.Bacc("TRN2", target_bir_lowering=False, num_devices=1)
    arrays, args = {}, []
    for name, a in laid_out.items():
        a = np.ascontiguousarray(a)
        arrays[f"{name}_dram"] = a
        args.append(nc.dram_tensor(f"{name}_dram", a.shape, mybir.dt.from_np(a.dtype), kind="ExternalInput").ap())
    out = nc.dram_tensor("out_dram", (B, S, D), F32, kind="ExternalOutput").ap()
    layers_kernel(nc, *args, out)
    result = run_bass_kernel_spmd(nc, [arrays], core_ids=[0])
    return result.results[0]["out_dram"]
```

```python
from contextlib import ExitStack

import concourse.bass as bass
from concourse import mybir
from concourse.alu_op_type import AluOpType as ALU

ACT = mybir.ActivationFunctionType
F32 = mybir.dt.float32
F32R = mybir.dt.float32r
I32 = mybir.dt.int32

P = 128
B, S, D = 8, 128, 512
C = D // P
R = 16
TAPS = 5
HALO = (TAPS - 1) // 2
G = 32
LOW = 3 * G
WARM_UPS = 11
DMA = 16


class Batch:

    def __init__(self, index, rounds, slot):
        self.index, self.rounds, self.slot = index, rounds, slot
        self.is_first = isinstance(index, int) and index == 0
        self.is_second = isinstance(index, int) and index == 1
        self.is_third = isinstance(index, int) and index == 2
        self.in_first_pair = isinstance(index, int) and index < 2

    def shift(self, by):
        moved = self.slot + by
        return Batch(self.index + by, self.rounds + moved // 2, moved % 2)


def fixed(n):
    return Batch(n, n // 2, n % 2)


def in_pair(pair, member):
    return Batch(2 * pair, pair, 0).shift(member)


def layers_kernel(nc, xT, len_dram, id0, id1, id3, w0T, bias0, ab0, w1T, conv_w, w3T, bias3, ab3, out):
    ctx = ExitStack()
    with ctx:
        def sb(name, shape, dt=F32):
            return ctx.enter_context(nc.sbuf_tensor(name, shape, dt))

        def psum(name):
            return ctx.enter_context(nc.psum_tensor(name, [P, D], F32))

        def sem(name):
            return ctx.enter_context(nc.semaphore(name))

        def sems(name, n):
            return [sem(f"{name}_{k}") for k in range(n)]

        x_raw = sb("x_raw", [P, 2, D])
        w0_raw = sb("w0_raw", [P, C, D])
        w1_raw = sb("w1_raw", [P, 2, C * D])
        w3_raw = sb("w3_raw", [P, C, D])
        ab_raw = [sb(f"ab{n}_raw", [P, 2, ab_dram.shape[2]]) for n, ab_dram in ((0, ab0), (3, ab3))]
        a_scaled = sb("a_scaled", [P, C, R])
        xT_hi, xT_lo = sb("xT_hi", [P, 2, D], F32R), sb("xT_lo", [P, 2, D], F32R)
        x1T_hi, x1T_lo = sb("x1T_hi", [P, D], F32R), sb("x1T_lo", [P, D], F32R)
        x2T_hi, x2T_lo = sb("x2T_hi", [P, D], F32R), sb("x2T_lo", [P, D], F32R)
        w0_hi, w0_lo = sb("w0_hi", [P, C, D], F32R), sb("w0_lo", [P, C, D], F32R)
        w1_hi, w1_lo = sb("w1_hi", [P, 2, C * D], F32R), sb("w1_lo", [P, 2, C * D], F32R)
        w3_hi, w3_lo = sb("w3_hi", [P, C, D], F32R), sb("w3_lo", [P, C, D], F32R)
        a_cat = [sb(f"a{n}_cat", [P, 2, C, 2, 2, R], F32R) for n in (0, 3)]
        b_cat = [sb(f"b{n}_cat", [LOW, 2, D], F32R) for n in (0, 3)]
        h_cat = [sb(f"h{n}_cat", [LOW, S], F32R) for n in (0, 3)]
        x1 = sb("x1", [P, 2, D])
        x2 = sb("x2", [P, D])
        masked = sb("masked", [P, D])
        x4 = sb("x4", [P, 2, D])
        identity_halo = sb("identity_halo", [P, P + 2 * HALO])
        identity = identity_halo[:, HALO:HALO + P]
        position = sb("position", [P, D])
        conv_taps = sb("conv_taps", [P, TAPS])
        band = sb("band", [P, P])
        bias3_rows = sb("bias3_rows", [P, D])
        bias0_rows = sb("bias0_rows", [P, D])
        warm_up = sb("warm_up", [P, D], F32R)
        length_int = sb("length_int", [P, B], I32)
        length = sb("length", [P, B])
        inv_length = sb("inv_length", [P, B])
        row_sum = sb("row_sum", [P, 1])
        gate = sb("gate", [P, 1])
        zero = sb("zero", [P, 1])
        gate_plus_1 = sb("gate_plus_1", [P, 1])

        ps_l0, ps_l1, ps_l3 = psum("ps_l0"), psum("ps_l1"), psum("ps_l3")
        ps_x1T, ps_x2T = psum("ps_x1T"), psum("ps_x2T")
        ps_low = [psum("ps_low0"), psum("ps_low3")]
        ps_conv = psum("ps_conv")

        x_loaded = sems("x_loaded", 2)
        w1_loaded = [sems("w1_first_half_loaded", 2), sems("w1_second_half_loaded", 2)]
        ab_loaded = [sems("ab0_loaded", 2), sems("ab3_loaded", 2)]
        first_ab0_loaded = sem("first_ab0_loaded")
        w0_loaded, w3_loaded = sems("w0_loaded", C), sems("w3_loaded", C)
        bias0_loaded, taps_and_lengths_loaded, bias3_loaded = sem("bias0_loaded"), sem("taps_and_lengths_loaded"), sem("bias3_loaded")
        stored = sems("stored", 2)
        zero_ready, warm_up_ready = sem("zero_ready"), sem("warm_up_ready")
        identity_zeroed, identity_ready, position_ready = sem("identity_zeroed"), sem("identity_ready"), sem("position_ready")
        length_ready, inv_length_ready, band_step = sem("length_ready"), sem("inv_length_ready"), sem("band_step")
        w0_plus_i, w0_hi_ready, w0_split = sem("w0_plus_i"), sem("w0_hi_ready"), sem("w0_split")
        w3_plus_i, w3_hi_ready, w3_split = sem("w3_plus_i"), sem("w3_hi_ready"), sem("w3_split")
        xT_hi_ready, xT_split = sem("xT_hi_ready"), sem("xT_split")
        w1_hi_ready, w1_split = sem("w1_hi_ready"), sem("w1_split")
        a3_scaled = sem("a3_scaled")
        a_hi_ready, b_hi_ready = [sem("a0_hi_ready"), sem("a3_hi_ready")], [sem("b0_hi_ready"), sem("b3_hi_ready")]
        a_split, b_split = [sem("a0_split"), sem("a3_split")], [sem("b0_split"), sem("b3_split")]
        low_done = [sem("low0_done"), sem("low3_done")]
        h_hi_ready, h_split = [sem("h0_hi_ready"), sem("h3_hi_ready")], [sem("h0_split"), sem("h3_split")]
        l0_done, l1_done, l3_done = sem("l0_done"), sem("l1_done"), sem("l3_done")
        x1_ready, x2_ready = sem("x1_ready"), sem("x2_ready")
        x1T_done, x1T_hi_ready, x1T_split = sem("x1T_done"), sem("x1T_hi_ready"), sem("x1T_split")
        x2T_done, x2T_hi_ready, x2T_split = sem("x2T_done"), sem("x2T_hi_ready"), sem("x2T_split")
        row_sum_ready, conv_done, gate_ready, gate_plus_ready = sem("row_sum_ready"), sem("conv_done"), sem("gate_ready"), sem("gate_plus_ready")
        x4_ready = sem("x4_ready")

        A_COLS, B_COLS = slice(0, C * R), slice(C * R, C * R + D)
        W1_HALVES = [slice(k * C * D // 2, (k + 1) * C * D // 2) for k in range(2)]

        def load_ab(eng, b, n):
            ids, ab_dram = ((id0, ab0), (id3, ab3))[n]
            which = eng.value_load(ids[0:1, bass.ds(b.index, 1)], min_val=0, max_val=ab_dram.shape[0] - 1)
            if not b.in_first_pair:
                eng.wait_ge(a_split[n], b.index - 1)
                eng.wait_ge(b_split[n], b.index - 1)
            eng.dma_start(ab_raw[n][:, b.slot, :], ab_dram[bass.ds(which, 1), :, :].rearrange("b p n -> (b p) n")).then_inc(
                first_ab0_loaded if b.is_first and n == 0 else ab_loaded[n][b.slot], DMA)

        def wait_ab(eng, b, n):
            if b.is_first and n == 0:
                eng.wait_ge(first_ab0_loaded, DMA)
            else:
                eng.wait_ge(ab_loaded[n][b.slot], DMA * (b.rounds + (0 if n == 0 and b.slot == 0 else 1)))

        HALVES = [slice(k * D // 2, (k + 1) * D // 2) for k in range(2)]

        def store_half(eng, half):
            eng.wait_ge(x4_ready, B + half)
            eng.dma_start(out[B - 1, :, HALVES[half]], x4[:, (B - 1) % 2, HALVES[half]]).then_inc(stored[(B - 1) % 2], DMA)

        block = ctx.enter_context(nc.Block())

        @block.sync
        def _(sp):
            def load_x(b):
                if not b.in_first_pair:
                    sp.wait_ge(xT_split, b.index - 1)
                sp.dma_start(x_raw[:, b.slot, :], xT[bass.ds(b.index, 1), :, :].rearrange("b p n -> (b p) n")).then_inc(x_loaded[b.slot], DMA)

            def load_w1(b):
                which = sp.value_load(id1[0:1, bass.ds(b.index, 1)], min_val=0, max_val=w1T.shape[0] - 1)
                for half, cols in enumerate(W1_HALVES):
                    if not b.in_first_pair:
                        sp.wait_ge(w1_split, 2 * (b.index - 2) + half + 1)
                    sp.dma_start(w1_raw[:, b.slot, cols], w1T[bass.ds(which, 1), :, cols].rearrange("b p n -> (b p) n")).then_inc(w1_loaded[half][b.slot], DMA)
                    if b.is_first and half == 0:
                        sp.dma_start(bias0_rows[:, :], bias0.partition_broadcast(P)).then_inc(bias0_loaded, DMA)

            def load_chunk(w_raw, w_dram, c, loaded):
                sp.dma_start(w_raw[:, c, :], w_dram[:, c * D:(c + 1) * D]).then_inc(loaded[c], DMA)

            load_x(fixed(0))
            for c in range(C):
                load_chunk(w0_raw, w0T, c, w0_loaded)
            load_w1(fixed(0))
            load_x(fixed(1))
            load_ab(sp, fixed(1), 0)
            load_ab(sp, fixed(0), 1)
            for c in range(C):
                load_chunk(w3_raw, w3T, c, w3_loaded)
            load_w1(fixed(1))
            sp.dma_start(bias3_rows[:, :], bias3.partition_broadcast(P)).then_inc(bias3_loaded, DMA)
            load_ab(sp, fixed(1), 1)
            with sp.Fori(1, B // 2) as j:
                for member in range(2):
                    b = in_pair(j, member)
                    load_x(b)
                    load_ab(sp, b, 0)
                    load_w1(b)
                    load_ab(sp, b, 1)
            store_half(sp, 1)

        @block.gpsimd
        def _(pool):
            nc.gpsimd.memset(identity_halo[:, :], 0.0).then_inc(identity_zeroed, 1)
            pool.wait_ge(identity_zeroed, 1)
            nc.gpsimd.affine_select(out=identity_halo[:, :], in_=identity_halo[:, :], compare_op=ALU.not_equal, fill=1.0,
                                    base=HALO, pattern=[[-1, P + 2 * HALO]], channel_multiplier=1).then_inc(identity_ready, 1)
            load_ab(pool, fixed(0), 0)

            def split_a(b, n):
                a_in = ab_raw[n][:, b.slot, A_COLS].rearrange("p (c r) -> p c r", c=C)
                a_hi, a_lo = a_cat[n][:, b.slot, :, :, 0, :], a_cat[n][:, b.slot, :, :, 1, :]
                wait_ab(pool, b, n)
                if n == 1:
                    if not b.is_first:
                        pool.wait_ge(a_split[n], b.index)
                    nc.gpsimd.tensor_tensor(a_scaled[:, :, :], a_in, ab_raw[n][:, b.slot, C * R + D:].unsqueeze(2).broadcast_to([P, C, R]),
                                            ALU.mult).then_inc(a3_scaled, 1)
                    pool.wait_ge(a3_scaled, b.index + 1)
                    a_in = a_scaled[:, :, :]
                a_in = a_in.unsqueeze(2).broadcast_to([P, C, 2, R])
                if not b.in_first_pair:
                    pool.wait_ge((l0_done, l3_done)[n], b.index - 1)
                nc.gpsimd.tensor_tensor(a_hi, a_in, zero[:, :].unsqueeze(2).unsqueeze(3).broadcast_to([P, C, 2, R]), ALU.add).then_inc(a_hi_ready[n], 1)
                pool.wait_ge(a_hi_ready[n], b.index + 1)
                nc.gpsimd.tensor_tensor(a_lo, a_in, a_hi.bitcast(F32), ALU.subtract).then_inc(a_split[n], 1)

            def split_b(b, n):
                b_in, b_lo = ab_raw[n][0:G, b.slot, B_COLS], b_cat[n][0:G, b.slot, :]
                pool.wait_ge(b_hi_ready[n], b.index + 1)
                nc.gpsimd.tensor_tensor(b_lo, b_in, b_lo.bitcast(F32), ALU.subtract).then_inc(b_split[n], 1)

            def add_identity(w_raw, c, loaded, done):
                diagonal = w_raw[:, c, c * P:(c + 1) * P]
                pool.wait_ge(loaded[c], DMA)
                nc.gpsimd.tensor_tensor(diagonal, diagonal, identity, ALU.add).then_inc(done, 1)

            pool.wait_ge(zero_ready, 1)
            pool.wait_ge(identity_ready, 1)
            for c in range(C):
                add_identity(w0_raw, c, w0_loaded, w0_plus_i)
            split_a(fixed(0), 0)
            split_b(fixed(0), 0)
            nc.gpsimd.iota(position[:, :], pattern=[[1, D]], base=0, channel_multiplier=0,
                           allow_small_or_imprecise_dtypes=True).then_inc(position_ready, 1)
            split_a(fixed(1), 0)
            for c in range(C):
                add_identity(w3_raw, c, w3_loaded, w3_plus_i)
            split_b(fixed(1), 0)
            split_a(fixed(0), 1)
            split_b(fixed(0), 1)
            pool.wait_ge(w3_hi_ready, C)
            pool.wait_ge(w3_split, C - 1)
            nc.gpsimd.tensor_tensor(w3_lo[:, C - 1, :], w3_raw[:, C - 1, :], w3_hi[:, C - 1, :].bitcast(F32), ALU.subtract).then_inc(w3_split, 1)
            split_a(fixed(1), 1)
            split_b(fixed(1), 1)
            with pool.Fori(1, B // 2) as j:
                for member in range(2):
                    for split in (split_a, split_b):
                        for n in range(2):
                            split(in_pair(j, member), n)

        @block.scalar
        def _(act):
            def x_hi(b):
                act.wait_ge(x_loaded[b.slot], DMA * (b.rounds + 1))
                if not b.in_first_pair:
                    act.wait_ge(l0_done, b.index - 1)
                nc.scalar.copy(xT_hi[:, b.slot, :], x_raw[:, b.slot, :]).then_inc(xT_hi_ready, 1)

            def w1_hi_half(b, half):
                act.wait_ge(w1_loaded[half][b.slot], DMA * (b.rounds + 1))
                if not b.in_first_pair:
                    act.wait_ge(l1_done, b.index - 1)
                cols = W1_HALVES[half]
                nc.scalar.copy(w1_hi[:, b.slot, cols], w1_raw[:, b.slot, cols]).then_inc(w1_hi_ready, 1)

            def b_hi(b, n):
                wait_ab(act, b, n)
                if not b.in_first_pair:
                    act.wait_ge((l0_done, l3_done)[n], b.index - 1)
                nc.scalar.copy(b_cat[n][:, b.slot, :], ab_raw[n][0:LOW, b.slot, B_COLS]).then_inc(b_hi_ready[n], 1)

            def h_hi(b, n):
                act.wait_ge(low_done[n], b.index + 1)
                nc.scalar.copy(h_cat[n][0:2 * G, :], ps_low[n][0:2 * G, 0:S]).then_inc(h_hi_ready[n], 1)

            def x1T_hi_part(b):
                act.wait_ge(x1T_done, b.index + 1)
                if not b.is_first:
                    act.wait_ge(l1_done, b.index)
                nc.scalar.copy(x1T_hi[:, :], ps_x1T[:, :]).then_inc(x1T_hi_ready, 1)

            def x2T_hi_part(b):
                act.wait_ge(x2T_done, b.index + 1)
                if not b.is_first:
                    act.wait_ge(l3_done, b.index)
                nc.scalar.copy(x2T_hi[:, :], ps_x2T[:, :]).then_inc(x2T_hi_ready, 1)

            def gate_rows(b):
                act.wait_ge(conv_done, b.index + 1)
                if b.is_first:
                    act.wait_ge(inv_length_ready, 1)
                else:
                    act.wait_ge(gate_plus_ready, b.index)
                nc.scalar.activation(gate[:, :], ps_conv[:, 0:1], ACT.Sigmoid,
                                     scale=inv_length[:, bass.ds(b.index, 1)]).then_inc(gate_ready, 1)

            def w_hi(c, hi, raw, plus_i, hi_ready):
                act.wait_ge(plus_i, c + 1)
                nc.scalar.copy(hi[:, c, :], raw[:, c, :]).then_inc(hi_ready, 1)

            def store(b):
                act.wait_ge(x4_ready, b.index + 1)
                act.dma_start(out[bass.ds(b.index, 1), :, :].rearrange("b s n -> (b s) n"), x4[:, b.slot, :]).then_inc(stored[b.slot], DMA)

            act.wait_ge(zero_ready, 1)
            nc.scalar.activation(gate[:, :], zero[:, :], ACT.Sigmoid)
            x_hi(fixed(0))
            act.dma_start(conv_taps[:, :], conv_w.partition_broadcast(P)).then_inc(taps_and_lengths_loaded, DMA)
            act.dma_start(length_int[:, :], len_dram.partition_broadcast(P)).then_inc(taps_and_lengths_loaded, DMA)
            for c in range(C):
                w_hi(c, w0_hi, w0_raw, w0_plus_i, w0_hi_ready)
            b_hi(fixed(0), 0)
            h_hi(fixed(0), 0)
            w1_hi_half(fixed(0), 0)
            w1_hi_half(fixed(0), 1)
            x1T_hi_part(fixed(0))
            x_hi(fixed(1))
            b_hi(fixed(1), 0)
            b_hi(fixed(0), 1)
            for c in range(C):
                w_hi(c, w3_hi, w3_raw, w3_plus_i, w3_hi_ready)

            def step(b):
                before, after = b.shift(-1), b.shift(1)
                is_last = isinstance(b.index, int) and b.index == B - 1
                h_hi(b, 0)
                if b.is_second:
                    w1_hi_half(b, 0)
                x2T_hi_part(before)
                if not b.is_second:
                    b_hi(b, 1)
                    if not is_last:
                        b_hi(after, 0)
                gate_rows(before)
                if b.is_second:
                    w1_hi_half(b, 1)
                elif not is_last:
                    w1_hi_half(after, 0)
                x1T_hi_part(b)
                h_hi(before, 1)
                if not is_last:
                    x_hi(after)
                    if b.is_second:
                        b_hi(b, 1)
                        b_hi(after, 0)
                        w1_hi_half(after, 0)
                    w1_hi_half(after, 1)
                    store(before)

            step(fixed(1))
            step(fixed(2))
            with act.Fori(1, B // 2 - 1) as j:
                for member in range(2):
                    step(in_pair(j, 1 + member))
            step(fixed(B - 1))
            x2T_hi_part(fixed(B - 1))
            gate_rows(fixed(B - 1))
            store(fixed(B - 2))
            h_hi(fixed(B - 1), 1)
            store_half(act, 0)
            act.wait_ge(stored[0], DMA * (B // 2))
            act.wait_ge(stored[1], DMA * (B // 2 + 1))

        @block.vector
        def _(dve):
            def subtract(out_, full, hi):
                return nc.vector.tensor_tensor(out_, full, hi.bitcast(F32), ALU.subtract)

            def x_lo(b):
                dve.wait_ge(xT_hi_ready, b.index + 1)
                subtract(xT_lo[:, b.slot, :], x_raw[:, b.slot, :], xT_hi[:, b.slot, :]).then_inc(xT_split, 1)

            def w1_lo_half(b, half):
                cols = W1_HALVES[half]
                dve.wait_ge(w1_hi_ready, 2 * b.index + half + 1)
                subtract(w1_lo[:, b.slot, cols], w1_raw[:, b.slot, cols], w1_hi[:, b.slot, cols]).then_inc(w1_split, 1)

            def h_lo(b, n):
                dve.wait_ge(h_hi_ready[n], b.index + 1)
                subtract(h_cat[n][2 * G:LOW, :], ps_low[n][G:2 * G, 0:S], h_cat[n][G:2 * G, :]).then_inc(h_split[n], 1)

            def add_bias0(b):
                dve.wait_ge(l0_done, b.index + 1)
                if b.is_first:
                    dve.wait_ge(bias0_loaded, DMA)
                if not b.in_first_pair:
                    dve.wait_ge(x2_ready, b.index - 1)
                nc.vector.tensor_tensor(x1[:, b.slot, :], ps_l0[:, :], bias0_rows[:, :], ALU.add).then_inc(x1_ready, 1)

            def x1T_lo_part(b):
                dve.wait_ge(x1T_hi_ready, b.index + 1)
                subtract(x1T_lo[:, :], ps_x1T[:, :], x1T_hi[:, :]).then_inc(x1T_split, 1)

            def x2T_lo_part(b):
                dve.wait_ge(x2T_hi_ready, b.index + 1)
                subtract(x2T_lo[:, :], ps_x2T[:, :], x2T_hi[:, :]).then_inc(x2T_split, 1)

            def sum_x2(b):
                dve.wait_ge(l1_done, b.index + 1)
                if not b.is_first:
                    dve.wait_ge(x2T_done, b.index)
                    dve.wait_ge(row_sum_ready, b.index)
                nc.vector.tensor_tensor(x2[:, :], ps_l1[:, :], x1[:, b.slot, :], ALU.add).then_inc(x2_ready, 1)
                if b.is_first:
                    dve.wait_ge(position_ready, 1)
                    dve.wait_ge(length_ready, 1)
                else:
                    dve.wait_ge(conv_done, b.index)
                dve.wait_ge(x2_ready, b.index + 1)
                nc.vector.scalar_tensor_tensor(out=masked[:, :], in0=position[:, :], scalar=length[:, bass.ds(b.index, 1)], in1=x2[:, :],
                                               op0=ALU.is_lt, op1=ALU.mult, accum_out=row_sum[:, :]).then_inc(row_sum_ready, 1)

            def open_gate(b):
                dve.wait_ge(gate_ready, b.index + 1)
                if not b.is_first:
                    dve.wait_ge(x4_ready, b.index)
                nc.vector.tensor_scalar(gate_plus_1[:, :], gate[:, :], 1.0, None, ALU.add).then_inc(gate_plus_ready, 1)
                dve.wait_ge(l3_done, b.index + 1)
                if b.is_first:
                    dve.wait_ge(bias3_loaded, DMA)
                if not b.in_first_pair:
                    dve.wait_ge(stored[b.slot], DMA * b.rounds)
                dve.wait_ge(gate_plus_ready, b.index + 1)

            def gated(b, ps, cols):
                nc.vector.scalar_tensor_tensor(out=x4[:, b.slot, cols], in0=ps[:, cols], scalar=gate_plus_1[:, 0:1], in1=bias3_rows[:, cols],
                                               op0=ALU.mult, op1=ALU.add).then_inc(x4_ready, 1)

            def result(b):
                open_gate(b)
                gated(b, ps_l3, slice(0, D))

            def last_result():
                open_gate(fixed(B - 1))
                for cols in HALVES:
                    gated(fixed(B - 1), ps_l0, cols)

            def w_lo(c, lo, raw, hi, hi_ready, split):
                dve.wait_ge(hi_ready, c + 1)
                subtract(lo[:, c, :], raw[:, c, :], hi[:, c, :]).then_inc(split, 1)

            def make_band():
                for t in range(TAPS):
                    ones_at = identity_halo[:, t:t + P]
                    if t == 0:
                        nc.vector.tensor_scalar(band[:, :], ones_at, conv_taps[:, 0:1], None, ALU.mult).then_inc(band_step, 1)
                    else:
                        dve.wait_ge(band_step, t)
                        nc.vector.scalar_tensor_tensor(out=band[:, :], in0=ones_at, scalar=conv_taps[:, t:t + 1], in1=band[:, :],
                                                       op0=ALU.mult, op1=ALU.add).then_inc(band_step, 1)

            nc.vector.memset(zero[:, :], 0.0).then_inc(zero_ready, 1)
            nc.vector.memset(warm_up[:, :].bitcast(F32), 0.0).then_inc(warm_up_ready, 1)
            x_lo(fixed(0))
            for c in range(C):
                w_lo(c, w0_lo, w0_raw, w0_hi, w0_hi_ready, w0_split)
            dve.wait_ge(identity_ready, 1)
            dve.wait_ge(taps_and_lengths_loaded, 2 * DMA)
            make_band()
            h_lo(fixed(0), 0)
            add_bias0(fixed(0))
            w1_lo_half(fixed(0), 0)
            w1_lo_half(fixed(0), 1)
            x1T_lo_part(fixed(0))
            nc.vector.tensor_copy(length[:, :], length_int[:, :]).then_inc(length_ready, 1)
            x_lo(fixed(1))
            dve.wait_ge(length_ready, 1)
            nc.vector.reciprocal(inv_length[:, :], length[:, :]).then_inc(inv_length_ready, 1)
            for c in range(2):
                w_lo(c, w3_lo, w3_raw, w3_hi, w3_hi_ready, w3_split)
            sum_x2(fixed(0))

            def step(b):
                before, after = b.shift(-1), b.shift(1)
                is_last = isinstance(b.index, int) and b.index == B - 1
                h_lo(b, 0)
                if b.is_second:
                    w_lo(2, w3_lo, w3_raw, w3_hi, w3_hi_ready, w3_split)
                x2T_lo_part(before)
                add_bias0(b)
                if b.is_third:
                    w1_lo_half(b, 1)
                if not b.is_second and not is_last:
                    w1_lo_half(after, 0)
                if b.is_second:
                    w1_lo_half(b, 0)
                    w1_lo_half(b, 1)
                h_lo(before, 1)
                x1T_lo_part(b)
                if not is_last:
                    x_lo(after)
                if not is_last:
                    result(before)
                if not is_last and not b.is_second:
                    w1_lo_half(after, 1)
                if b.is_second:
                    w1_lo_half(after, 0)
                sum_x2(b)

            step(fixed(1))
            step(fixed(2))
            with dve.Fori(1, B // 2 - 1) as j:
                for member in range(2):
                    step(in_pair(j, 1 + member))
            step(fixed(B - 1))
            result(fixed(B - 2))
            x2T_lo_part(fixed(B - 1))
            h_lo(fixed(B - 1), 1)
            last_result()

        @block.tensor
        def _(pe):
            def low_rank(b, n, hi, lo):
                pe.wait_ge(a_split[n], b.index + 1)
                for c in range(C):
                    a = a_cat[n][:, b.slot, c, :, :, :].rearrange("p g k r -> p (g k r)")
                    for k, part in enumerate((hi, lo)):
                        last = nc.tensor.matmul(ps_low[n][0:2 * G, 0:S], a, part[:, c * P:(c + 1) * P],
                                                start=(c == 0 and k == 0), stop=(c == C - 1 and k == 1))
                last.then_inc(low_done[n], 1)

            def multiply_hi(ps, c, hi, w_hi_, w_lo_):
                rows, cols = slice(c * P, (c + 1) * P), slice(c * D, (c + 1) * D)
                nc.tensor.matmul(ps[:, :], hi[:, rows], w_hi_[:, cols], start=(c == 0), stop=False)
                nc.tensor.matmul(ps[:, :], hi[:, rows], w_lo_[:, cols], start=False, stop=False)

            def multiply_lo(ps, lo, w_hi_, stops):
                for c in range(C):
                    last = nc.tensor.matmul(ps[:, :], lo[:, c * P:(c + 1) * P], w_hi_[:, c * D:(c + 1) * D],
                                            start=False, stop=(stops and c == C - 1))
                return last

            def add_low_rank(b, n, ps):
                pe.wait_ge(b_split[n], b.index + 1)
                pe.wait_ge(h_split[n], b.index + 1)
                return nc.tensor.matmul(ps[:, :], h_cat[n][:, :], b_cat[n][:, b.slot, :], start=False, stop=True)

            def transposes(ps, rows, done):
                for c in range(C):
                    last = nc.tensor.transpose(ps[:, c * P:(c + 1) * P], rows[:, c * P:(c + 1) * P], identity)
                last.then_inc(done, 1)

            w0 = [w[:, :, :].rearrange("p c n -> p (c n)") for w in (w0_hi, w0_lo)]
            w3 = [w[:, :, :].rearrange("p c n -> p (c n)") for w in (w3_hi, w3_lo)]

            def transpose_x1(b):
                pe.wait_ge(x1_ready, b.index + 1)
                transposes(ps_x1T, x1[:, b.slot, :], x1T_done)

            def transpose_x2(b):
                pe.wait_ge(x2_ready, b.index + 1)
                transposes(ps_x2T, x2, x2T_done)

            def layer0(b, between):
                hi, lo = xT_hi[:, b.slot, :], xT_lo[:, b.slot, :]
                pe.wait_ge(xT_split, b.index + 1)
                if not b.is_first:
                    low_rank(b, 0, hi, lo)
                for c in range(C):
                    if b.is_first:
                        pe.wait_ge(w0_split, c + 1)
                    multiply_hi(ps_l0, c, hi, *w0)
                    if c == C // 2:
                        between()
                if b.is_first:
                    low_rank(b, 0, hi, lo)
                multiply_lo(ps_l0, lo, w0[0], stops=False)
                add_low_rank(b, 0, ps_l0).then_inc(l0_done, 1)

            def convolve(b):
                pe.wait_ge(row_sum_ready, b.index + 1)
                if b.is_first:
                    pe.wait_ge(band_step, TAPS)
                else:
                    pe.wait_ge(gate_ready, b.index)
                nc.tensor.matmul(ps_conv[:, 0:1], band[:, :], row_sum[:, :], start=True, stop=True).then_inc(conv_done, 1)

            def layer3_start(b, ps, between):
                pe.wait_ge(x2T_hi_ready, b.index + 1)
                for c in range(C):
                    if b.is_first:
                        pe.wait_ge(w3_split, c + 1)
                    multiply_hi(ps, c, x2T_hi, *w3)
                    if c == C // 2 - 1:
                        between()
                pe.wait_ge(x2T_split, b.index + 1)
                low_rank(b, 1, x2T_hi, x2T_lo)

            def layer3(b, between):
                convolve(b)
                if not b.is_first:
                    pe.wait_ge(x4_ready, b.index)
                layer3_start(b, ps_l3, between)
                multiply_lo(ps_l3, x2T_lo, w3[0], stops=False)
                add_low_rank(b, 1, ps_l3).then_inc(l3_done, 1)

            def layer1(b):
                w1 = [w[:, b.slot, :] for w in (w1_hi, w1_lo)]
                pe.wait_ge(x1T_hi_ready, b.index + 1)
                for c in range(C):
                    if c % (C // 2) == 0:
                        pe.wait_ge(w1_split, 2 * b.index + c // (C // 2) + 1)
                    multiply_hi(ps_l1, c, x1T_hi, *w1)
                pe.wait_ge(x1T_split, b.index + 1)
                multiply_lo(ps_l1, x1T_lo, w1[0], stops=True).then_inc(l1_done, 1)

            def warm_ups(n):
                for _ in range(n):
                    nc.tensor.matmul(ps_x2T[:, :], warm_up[:, 0:P], warm_up[:, :], start=True, stop=True)

            pe.wait_ge(warm_up_ready, 1)
            warm_ups(WARM_UPS)

            layer0(fixed(0), lambda: None)
            warm_ups(4)
            transpose_x1(fixed(0))
            warm_ups(4)
            layer1(fixed(0))

            def step(b):
                before = b.shift(-1)
                layer0(b, lambda: transpose_x2(before))
                layer3(before, lambda: transpose_x1(b))
                layer1(b)

            step(fixed(1))
            step(fixed(2))
            with pe.Fori(1, B // 2 - 1) as j:
                for member in range(2):
                    step(in_pair(j, 1 + member))
            last, before = fixed(B - 1), fixed(B - 2)
            layer0(last, lambda: transpose_x2(before))
            convolve(before)
            pe.wait_ge(x4_ready, B - 2)
            layer3_start(before, ps_l3, lambda: transpose_x1(last))
            layer1(last)
            multiply_lo(ps_l3, x2T_lo, w3[0], stops=False)
            transpose_x2(last)
            add_low_rank(before, 1, ps_l3).then_inc(l3_done, 1)
            convolve(last)
            pe.wait_ge(x1_ready, B)
            layer3_start(last, ps_l0, lambda: None)
            multiply_lo(ps_l0, x2T_lo, w3[0], stops=False)
            add_low_rank(last, 1, ps_l0).then_inc(l3_done, 1)


def kernel(**inputs):
    import numpy as np
    import concourse.bacc as bacc
    from concourse.bass_utils import run_bass_kernel_spmd

    given = {name: np.asarray(a) for name, a in inputs.items()}

    def row(a):
        return a.reshape(1, -1)

    def features_first(w):
        *lead, rows, _ = w.shape
        w = w.reshape(*lead, rows, C, P)
        k = len(lead)
        return w.transpose(*range(k), k + 2, k + 1, k).reshape(*lead, P, C * rows)

    def low_rank(a, b, *scales):
        n = a.shape[0]
        b = np.tile(b.transpose(0, 2, 1), (1, LOW // R, 1))
        b = np.concatenate([b, np.zeros((n, P - LOW, D), b.dtype)], axis=1)
        return np.concatenate([features_first(a), b, *(np.tile(s.reshape(n, 1, 1), (1, P, 1)) for s in scales)], axis=2)

    laid_out = {
        "xT": features_first(given["x"]),
        "lengths": row(given["itok_B_9_3973"]),
        "id0": row(given["itok_B_6_15"]),
        "id1": row(given["itok_B_0_15"]),
        "id3": row(given["itok_B_1_7"]),
        "w0T": features_first(given["L0_cond_base_weight"]),
        "bias0": row(given["L0_cond_base_bias"]),
        "ab0": low_rank(given["L0_cond_lora_A_w"], given["L0_cond_lora_B_w"]),
        "w1T": features_first(given["L1_cond_weight"]),
        "conv_w": row(given["L2_cond_conv_w"]),
        "w3T": features_first(given["L3_cond_weight"]),
        "bias3": row(given["L3_cond_bias"]),
        "ab3": low_rank(given["L3_cond_lora_a_weights"], given["L3_cond_lora_b_weights"], given["L3_cond_scaling_factors"]),
    }
    nc = bacc.Bacc("TRN2", target_bir_lowering=False, num_devices=1)
    arrays, args = {}, []
    for name, a in laid_out.items():
        a = np.ascontiguousarray(a)
        arrays[f"{name}_dram"] = a
        args.append(nc.dram_tensor(f"{name}_dram", a.shape, mybir.dt.from_np(a.dtype), kind="ExternalInput").ap())
    out = nc.dram_tensor("out_dram", (B, S, D), F32, kind="ExternalOutput").ap()
    layers_kernel(nc, *args, out)
    result = run_bass_kernel_spmd(nc, [arrays], core_ids=[0])
    return result.results[0]["out_dram"]
```
